# Optimizing a Trainium2 kernel written in Bass

```python
import numpy as np
import jax
import jax.numpy as jnp

def _softmax(x, axis=-1):
    return jax.nn.softmax(x, axis=axis)

def _gelu(x):
    return jax.nn.gelu(x, approximate=True)

def _silu(x):
    return jax.nn.silu(x)

def _sigmoid(x):
    return jax.nn.sigmoid(x)

def _layernorm(x, axis=-1, eps=1e-05):
    m = jnp.mean(x, axis=axis, keepdims=True)
    v = jnp.var(x, axis=axis, keepdims=True)
    return (x - m) / jnp.sqrt(v + eps)

def _scatter_add(tgt, idx, src, axis=0):
    return tgt.at[idx].add(src)

def _segment_sum(src, seg, n):
    return jax.ops.segment_sum(src, seg, n)
kernel_name = 'mk_gnn_preln_d2_gnn_r8_336578'

def setup_inputs(seed: int=0):
    np.random.seed(seed)
    _w = jnp.asarray

    def _rec_inputs():
        import jax
        import jax.numpy as jnp
        _gk = jax.random.key(seed)
        x = -0.000202 + 1 * jax.random.normal(jax.random.fold_in(_gk, 1), (6250, 128), jnp.float32)
        src = jax.random.randint(jax.random.fold_in(_gk, 2), (100000,), 0, 6250, jnp.int32)
        dst = jax.random.randint(jax.random.fold_in(_gk, 3), (100000,), 0, 6250, jnp.int32)
        _o = jnp.argsort(dst, stable=True)
        src = src[_o]
        dst = dst[_o]
        edge_attr_128 = -4.21973e-05 + 0.999841 * jax.random.normal(jax.random.fold_in(_gk, 12), (100000, 128), jnp.float32)
        return (x, src, dst, edge_attr_128)
    x, src, dst, edge_attr_128 = _rec_inputs()

    def _L0_gnn_setup():
        import jax, jax.numpy as jnp
        import numpy as np
        N = 6250
        E = 75000
        D = 128
        G = 64
        GN_EPS = 1e-05

        def graph_norm(x, batch, weight, bias, mean_scale):
            ones = jnp.ones((x.shape[0],), dtype=x.dtype)
            cnt = jnp.maximum(jax.ops.segment_sum(ones, batch, num_segments=G), 1.0)[:, None]
            mean = jax.ops.segment_sum(x, batch, num_segments=G) / cnt
            out = x - mean[batch] * mean_scale
            var = jax.ops.segment_sum(out * out, batch, num_segments=G) / cnt
            std = jnp.sqrt(var + GN_EPS)
            return weight * out / std[batch] + bias
        key = jax.random.key(seed)
        ks = jax.random.split(key, 10)
        node_h = jax.random.normal(ks[0], (N, D), dtype=jnp.float32)
        edge_attr = jax.random.normal(ks[1], (E, D), dtype=jnp.float32)
        batch = jnp.sort(jax.random.randint(ks[2], (N,), 0, G)).astype(jnp.int64)
        edge_index = jax.random.randint(ks[3], (2, E), 0, N).astype(jnp.int64)
        w1 = jax.random.normal(ks[4], (D, D), dtype=jnp.float32) * 0.02
        b1 = jnp.zeros((D,), dtype=jnp.float32)
        we = jax.random.normal(ks[5], (D, D), dtype=jnp.float32) * 0.02
        be = jnp.zeros((D,), dtype=jnp.float32)
        eps = jnp.zeros((), dtype=jnp.float32)
        gn_weight = jnp.ones((D,), dtype=jnp.float32)
        gn_bias = jnp.zeros((D,), dtype=jnp.float32)
        gn_mean_scale = jnp.ones((D,), dtype=jnp.float32)
        return {'node_h': node_h, 'edge_attr': edge_attr, 'batch': batch, 'edge_index': edge_index, 'w1': w1, 'b1': b1, 'we': we, 'be': be, 'eps': eps, 'gn_weight': gn_weight, 'gn_bias': gn_bias, 'gn_mean_scale': gn_mean_scale}
    _L0_gnn_all = _L0_gnn_setup()
    _L0_gnn_in = {k: v for k, v in _L0_gnn_all.items() if k in ('w1', 'b1', 'we', 'be', 'eps', 'gn_weight', 'gn_bias', 'gn_mean_scale')}
    del _L0_gnn_all

    def _L1_gnn_setup():
        import jax, jax.numpy as jnp
        import numpy as np
        N, E = (12500, 200000)
        IN_CH, HID, HEADS = (128, 64, 2)
        NEG_SLOPE = 0.2

        def gat_layer(x, edge_index, W, a_src, a_dst, b):
            n = x.shape[0]
            H, C = a_src.shape
            loop = jnp.arange(n, dtype=edge_index.dtype)
            src = jnp.concatenate([edge_index[0], loop])
            dst = jnp.concatenate([edge_index[1], loop])
            h = (x @ W).reshape(n, H, C)
            alpha_src = (h * a_src[None]).sum(-1)
            alpha_dst = (h * a_dst[None]).sum(-1)
            e = jax.nn.leaky_relu(alpha_src[src] + alpha_dst[dst], NEG_SLOPE)
            m = jax.ops.segment_max(e, dst, num_segments=n)
            e = jnp.exp(e - m[dst])
            s = jax.ops.segment_sum(e, dst, num_segments=n)
            alpha = e / s[dst]
            msg = h[src] * alpha[..., None]
            out = jax.ops.segment_sum(msg, dst, num_segments=n)
            return out.reshape(n, H * C) + b
        key = jax.random.key(seed)
        ks = jax.random.split(key, 12)
        x = jax.random.normal(ks[0], (N, IN_CH), dtype=jnp.float32)
        edge_index = jax.random.randint(ks[1], (2, E), 0, N, dtype=jnp.int64)
        d1 = HEADS * HID
        W1 = jax.random.normal(ks[2], (IN_CH, d1), dtype=jnp.float32) * 0.05
        a_src1 = jax.random.normal(ks[3], (HEADS, HID), dtype=jnp.float32) * 0.05
        a_dst1 = jax.random.normal(ks[4], (HEADS, HID), dtype=jnp.float32) * 0.05
        b1 = jnp.zeros((d1,), dtype=jnp.float32)
        W2 = jax.random.normal(ks[5], (d1, d1), dtype=jnp.float32) * 0.05
        a_src2 = jax.random.normal(ks[6], (HEADS, HID), dtype=jnp.float32) * 0.05
        a_dst2 = jax.random.normal(ks[7], (HEADS, HID), dtype=jnp.float32) * 0.05
        b2 = jnp.zeros((d1,), dtype=jnp.float32)
        return {'x': x, 'edge_index': edge_index, 'W1': W1, 'a_src1': a_src1, 'a_dst1': a_dst1, 'b1': b1, 'W2': W2, 'a_src2': a_src2, 'a_dst2': a_dst2, 'b2': b2}
    _L1_gnn_all = _L1_gnn_setup()
    _L1_gnn_in = {k: v for k, v in _L1_gnn_all.items() if k in ('W1', 'a_src1', 'a_dst1', 'b1', 'W2', 'a_src2', 'a_dst2', 'b2')}
    del _L1_gnn_all
    return {'x': x, 'src': src, 'dst': dst, 'edge_attr_128': edge_attr_128, 'L0_gnn_w1': _L0_gnn_in['w1'], 'L0_gnn_b1': _L0_gnn_in['b1'], 'L0_gnn_we': _L0_gnn_in['we'], 'L0_gnn_be': _L0_gnn_in['be'], 'L0_gnn_eps': _L0_gnn_in['eps'], 'L0_gnn_gn_weight': _L0_gnn_in['gn_weight'], 'L0_gnn_gn_bias': _L0_gnn_in['gn_bias'], 'L0_gnn_gn_mean_scale': _L0_gnn_in['gn_mean_scale'], 'L1_gnn_W1': _L1_gnn_in['W1'], 'L1_gnn_a_src1': _L1_gnn_in['a_src1'], 'L1_gnn_a_dst1': _L1_gnn_in['a_dst1'], 'L1_gnn_b1': _L1_gnn_in['b1'], 'L1_gnn_W2': _L1_gnn_in['W2'], 'L1_gnn_a_src2': _L1_gnn_in['a_src2'], 'L1_gnn_a_dst2': _L1_gnn_in['a_dst2'], 'L1_gnn_b2': _L1_gnn_in['b2']}

def reference(x, src, dst, edge_attr_128, L0_gnn_w1, L0_gnn_b1, L0_gnn_we, L0_gnn_be, L0_gnn_eps, L0_gnn_gn_weight, L0_gnn_gn_bias, L0_gnn_gn_mean_scale, L1_gnn_W1, L1_gnn_a_src1, L1_gnn_a_dst1, L1_gnn_b1, L1_gnn_W2, L1_gnn_a_src2, L1_gnn_a_dst2, L1_gnn_b2):
    import jax
    import jax.numpy as jnp

    def _L0_gnn_ref(node_h, edge_attr, batch, edge_index, w1, b1, we, be, eps, gn_weight, gn_bias, gn_mean_scale):
        import jax, jax.numpy as jnp
        import numpy as np
        N = 6250
        E = 75000
        D = 128
        G = 64
        GN_EPS = 1e-05

        def graph_norm(x, batch, weight, bias, mean_scale):
            ones = jnp.ones((x.shape[0],), dtype=x.dtype)
            cnt = jnp.maximum(jax.ops.segment_sum(ones, batch, num_segments=G), 1.0)[:, None]
            mean = jax.ops.segment_sum(x, batch, num_segments=G) / cnt
            out = x - mean[batch] * mean_scale
            var = jax.ops.segment_sum(out * out, batch, num_segments=G) / cnt
            std = jnp.sqrt(var + GN_EPS)
            return weight * out / std[batch] + bias
        h = node_h @ w1.T + b1
        src, dst = (edge_index[0], edge_index[1])
        msg = jax.nn.silu(h[src] + (edge_attr @ we.T + be))
        agg = jax.ops.segment_sum(msg, dst, num_segments=N)
        conv = (1.0 + eps) * h + agg
        out = jax.nn.silu(conv)
        return graph_norm(out + node_h, batch, gn_weight, gn_bias, gn_mean_scale)

    def _L1_gnn_ref(x, edge_index, W1, a_src1, a_dst1, b1, W2, a_src2, a_dst2, b2):
        import jax, jax.numpy as jnp
        import numpy as np
        N, E = (12500, 200000)
        IN_CH, HID, HEADS = (128, 64, 2)
        NEG_SLOPE = 0.2

        def gat_layer(x, edge_index, W, a_src, a_dst, b):
            n = x.shape[0]
            H, C = a_src.shape
            loop = jnp.arange(n, dtype=edge_index.dtype)
            src = jnp.concatenate([edge_index[0], loop])
            dst = jnp.concatenate([edge_index[1], loop])
            h = (x @ W).reshape(n, H, C)
            alpha_src = (h * a_src[None]).sum(-1)
            alpha_dst = (h * a_dst[None]).sum(-1)
            e = jax.nn.leaky_relu(alpha_src[src] + alpha_dst[dst], NEG_SLOPE)
            m = jax.ops.segment_max(e, dst, num_segments=n)
            e = jnp.exp(e - m[dst])
            s = jax.ops.segment_sum(e, dst, num_segments=n)
            alpha = e / s[dst]
            msg = h[src] * alpha[..., None]
            out = jax.ops.segment_sum(msg, dst, num_segments=n)
            return out.reshape(n, H * C) + b
        h = gat_layer(x, edge_index, W1, a_src1, a_dst1, b1)
        h = jax.nn.elu(h)
        h = gat_layer(h, edge_index, W2, a_src2, a_dst2, b2)
        h = jax.nn.elu(h)
        return h
    edge_index = jnp.stack([src, dst])
    batch0 = jnp.zeros((6250,), jnp.int32)
    h = jnp.maximum(_layernorm(x, axis=-1), 0.0)
    x = x + _L0_gnn_ref(h, edge_attr_128, batch0, edge_index, L0_gnn_w1, L0_gnn_b1, L0_gnn_we, L0_gnn_be, L0_gnn_eps, L0_gnn_gn_weight, L0_gnn_gn_bias, L0_gnn_gn_mean_scale)
    h = jnp.maximum(_layernorm(x, axis=-1), 0.0)
    x = x + _L1_gnn_ref(h, edge_index, L1_gnn_W1, L1_gnn_a_src1, L1_gnn_a_dst1, L1_gnn_b1, L1_gnn_W2, L1_gnn_a_src2, L1_gnn_a_dst2, L1_gnn_b2)
    return x

_drawn_inputs = setup_inputs


def setup_inputs(seed=0):
    import zlib

    import numpy as np

    out = dict(_drawn_inputs(seed))
    spreads = {'L0_gnn_b1': (0.0, 0.1),
     'L0_gnn_be': (0.0, 0.1),
     'L0_gnn_gn_weight': (1.0, 0.2),
     'L0_gnn_gn_bias': (0.0, 0.1),
     'L0_gnn_gn_mean_scale': (1.0, 0.2),
     'L1_gnn_b1': (0.0, 0.277),
     'L1_gnn_b2': (0.0, 0.1)}
    factors = {'L1_gnn_a_src1': 27.168,
     'L1_gnn_a_dst1': 200.0,
     'L1_gnn_a_src2': 64.0,
     'L1_gnn_a_dst2': 200.0}
    for name, (base, spread) in spreads.items():
        noise = np.random.default_rng([zlib.crc32(name.encode()), seed]).standard_normal(out[name].shape)
        drawn = base * np.exp(spread * noise) if base else spread * noise
        out[name] = jnp.asarray(drawn.astype(out[name].dtype))
    for name, factor in factors.items():
        out[name] = (out[name] * factor).astype(out[name].dtype)
    return out
```

```python
from contextlib import ExitStack, contextmanager

import concourse.bass as bass
from concourse import mybir

F32 = mybir.dt.float32
BF16 = mybir.dt.bfloat16
I32 = mybir.dt.int32
I16 = mybir.dt.int16
ALU = mybir.AluOpType
ACT = mybir.ActivationFunctionType
AX = mybir.AxisListType
ds = bass.ds

P = 128
N = 6250
E = 100000
D = 128
HEADS = 2
HID = D // HEADS
WINDOWS = -(-N // P)
TAIL = N - (WINDOWS - 1) * P
K = 4
EG = P * K
GROUPS = -(-E // EG)
STEPS = GROUPS + WINDOWS - 1
LAST_EDGE = E - EG
REPEATED = GROUPS * EG - E
NOWHERE = WINDOWS * P - 1
HALF_G = GROUPS // 2
RING = 14
HALF_R = RING // 2
ROUNDS = GROUPS // RING
IN_FLIGHT = 2
CH = 7
CHUNKS = WINDOWS // CH
ROW = D + HEADS + 3
SLOT = 136
AUG = D + 2 * HEADS
UNROLL = 4
SKIP = 8
FAR = 2.0 ** 100
LN_EPS = 1e-5
GN_EPS = 1e-5
SLOPE = 0.2
assert GROUPS == ROUNDS * RING and WINDOWS == CHUNKS * CH and STEPS % UNROLL == 0


def past(s, n):
    return not isinstance(s, int) or s >= n


def run_steps(eng, stages):
    most = max(lag for _, lag in stages)
    assert most <= SKIP
    for t in range(SKIP):
        for fn, lag in stages:
            if t >= lag:
                fn(t - lag, (t - lag) % UNROLL, (t - lag) // UNROLL)
    with eng.Fori(SKIP // UNROLL, STEPS // UNROLL) as i:
        for u in range(UNROLL):
            for fn, lag in stages:
                fn(i * UNROLL + (u - lag), (u - lag) % UNROLL, i + (u - lag) // UNROLL)
    for t in range(STEPS, STEPS + most):
        for fn, lag in stages:
            if t - lag < STEPS:
                fn(t - lag, (t - lag) % UNROLL, (t - lag) // UNROLL)


class Own:

    def __init__(self, eng, sem):
        self.eng, self.sem, self.n = eng, sem, 0

    def __call__(self, instruction):
        instruction.then_inc(self.sem, 1)
        self.n = self.n + 1
        self.eng.wait_ge(self.sem, self.n)

    @contextmanager
    def loop(self, start, end, each):
        before = self.n
        with self.eng.Fori(start, end) as i:
            self.n = i * each + (before - start * each)
            yield i
        self.n = before + (end - start) * each


def gnn_kernel(nc, x, src, dst, edge_attr_128, L0_gnn_w1, L0_gnn_b1, L0_gnn_we, L0_gnn_be, L0_gnn_eps,
               L0_gnn_gn_weight, L0_gnn_gn_bias, L0_gnn_gn_mean_scale,
               L1_gnn_W1, L1_gnn_a_src1, L1_gnn_a_dst1, L1_gnn_b1,
               L1_gnn_W2, L1_gnn_a_src2, L1_gnn_a_dst2, L1_gnn_b2, out):
    ctx = ExitStack()
    with ctx:
        def sb(name, shape, dt=F32):
            return ctx.enter_context(nc.sbuf_tensor(name, shape, dt))

        def sem(name):
            return ctx.enter_context(nc.semaphore(name))

        conv_table = nc.dram_tensor("conv_table", (WINDOWS * P, D), F32).ap()
        gat_tables = [nc.dram_tensor(f"gat_table{n}", (WINDOWS * P, ROW), F32).ap() for n in range(2)]
        dst_rows = nc.dram_tensor("dst_rows", (GROUPS * EG,), I16).ap()

        x_sb = sb("x_sb", [P, WINDOWS, D])
        h_sb = sb("h_sb", [P, WINDOWS, D])
        hw_sb = sb("hw_sb", [P, WINDOWS, D])
        acc = sb("acc", [P, WINDOWS, HEADS * (HID + 1)])
        acc_heads = acc[:, :, :].rearrange("p w (h c) -> p w h c", h=HEADS)
        node_scores = sb("node_scores", [P, WINDOWS, 2 * HEADS])

        rows = sb("rows", [P, RING, K, ROW])
        iota_node = sb("iota_node", [P, WINDOWS * P], I16)
        src_idx = sb("src_idx", [P, GROUPS * K], I32)
        dst_col = sb("dst_col", [P, GROUPS * K])
        idx_stage = sb("idx_stage", [P, 2, HALF_R * K], I32)
        four = sb("four", [P, UNROLL, EG])
        edge_in = four
        onehot_t = four
        two_a = sb("two_a", [P, 2, EG])
        edge_t = two_a
        far = two_a
        two_b = sb("two_b", [P, 2, EG])
        pre_act = two_b
        masked = two_b
        onehot = sb("onehot", [P, UNROLL, K, P])
        msg = sb("msg", [P, UNROLL, K, HEADS * (HID + 1)])
        msg_heads = msg[:, :, :, :].rearrange("p b k (h c) -> p b k h c", h=HEADS)
        dst_bc = sb("dst_bc", [P, UNROLL, EG], I16)
        parts = sb("parts", [P, 2, K * HEADS * 3], BF16)
        parts_t = sb("parts_t", [K * HEADS * 3, 2, P], BF16)
        step_rhs = sb("step_rhs", [P, UNROLL, 2 * HEADS])
        local_max = sb("local_max", [P, 2, HEADS])
        tmp_m = sb("tmp_m", [P, 2, 3, HEADS])
        score = sb("score", [P, 2, 3, K * HEADS])
        logit = sb("logit", [P, UNROLL, K * HEADS])
        shrink_log = sb("shrink_log", [P, UNROLL, HEADS])
        shrink = sb("shrink", [P, UNROLL, HEADS])

        ident = sb("ident", [P, P])
        ident_bf = sb("ident_bf", [P, P], BF16)
        ones = sb("ones", [P, P])
        ones_tail = sb("ones_tail", [P, P])
        pick = sb("pick", [K * HEADS * 3, K * HEADS, P], BF16)
        one_col = sb("one_col", [P, 1])
        far_node = sb("far_node", [P, WINDOWS])
        sched = sb("sched", [1, STEPS], I32)
        window_of = sb("window_of", [1, STEPS], I32)
        first_edge = sb("first_edge", [1, STEPS], I32)
        freed_at = sb("freed_at", [1, GROUPS], I32)
        w1_t = sb("w1_t", [P, D])
        we_t = sb("we_t", [P, D])
        aug = sb("aug", [P, 2, AUG])
        head_w = sb("head_w", [P, 2, 2 * HEADS])
        w_raw = sb("w_raw", [P, 2, D])
        w2_t = sb("w2_t", [P, 2, D])
        vec = sb("vec", [P, 7, D])
        B1, BE, GNW, GNB, GNMS, GB1, GB2 = range(7)
        one_eps = sb("one_eps", [P, 1])
        cvec = sb("cvec", [P, 6, D])
        stats = sb("stats", [P, 8, CH])
        gat_stats = sb("gat_stats", [P, CH, HEADS])
        gat_tmp = sb("gat_tmp", [P, 2, CH, HEADS])

        flat_rows = rows[:, :, :, :].rearrange("p r k c -> p (r k c)")
        T1, T2, FEAT, FEAT_T = (flat_rows[:, i * CH * D:(i + 1) * CH * D].rearrange("p (w c) -> p w c", c=D)
                                for i in range(4))
        STAGE = flat_rows[:, 4 * CH * D:4 * CH * D + CH * ROW]
        stage_conv = STAGE[:, 0:CH * D].rearrange("p (w c) -> p w c", c=D)
        stage_gat = STAGE.rearrange("p (w c) -> p w c", c=ROW)
        stage_parts = STAGE.bitcast(BF16).rearrange("p (w c) -> p w c", c=2 * ROW)[:, :, 2 * (D + HEADS):]
        stage_parts = stage_parts.rearrange("p w (h c) -> p w h c", h=HEADS)

        def prep(i, dt=F32):
            a = acc[:, :, :].rearrange("p w c -> p (w c)")[0:HALF_G, i * 2 * EG:(i + 1) * 2 * EG]
            return (a if dt is F32 else a.bitcast(dt)).rearrange("g (b e) -> g b e", b=2)
        src_g, dst_g, srcf_g, dstf_g = prep(0, I32), prep(1, I32), prep(2), prep(3)
        dst16_g = acc[:, :, :].rearrange("p w c -> p (w c)")[0:HALF_G, 8 * EG:9 * EG].bitcast(I16) \
            .rearrange("g (b e) -> g b e", b=2)
        step128 = acc[:, :, :].rearrange("p w c -> p (w c)")[0:HALF_G, 9 * EG:9 * EG + STEPS]
        past_g = acc[:, :, :].rearrange("p w c -> p (w c)")[0:HALF_G, 10 * EG:10 * EG + 2 * STEPS] \
            .rearrange("g (b s) -> g b s", b=2)
        reach = acc[:, :, :].rearrange("p w c -> p (w c)")[0:HALF_G, 11 * EG:11 * EG + 8]

        bank = [ctx.enter_context(nc.psum_tensor(f"bank{i}", [P, 512], F32)) for i in range(7)]
        bank_bf = ctx.enter_context(nc.psum_tensor("bank_bf", [P, 1024], BF16))
        trans_ps = [bank[0], bank[1]]
        edge_ps = [bank[2], bank[3]]
        agg_ps = [bank[4], bank[5]]
        score_ps = [[bank[0], bank[1]], [bank[2], bank[3]]]
        exp_ps = bank[6]

        def proj(j0, n, cols):
            return bank[2 + j0 // 3][:, 0:n * SLOT].rearrange("p (t c) -> p t c", c=SLOT)[:, :, cols]
        PROJ = [(0, 3), (3, 3), (6, 1)]

        names = """norm_begun x_loaded params_loaded edges_loaded dst_rows_stored filled consts ids_ready edgef_ready
            dst16_ready edge_t_ready idx_ready reach_ready past_ready sched_ps sched_ready
            w_trans w_trans_copied head_ready aug_ps aug_ready
            centred squared variance std scaled feat_ready feat_trans feat_copied projected evacuated
            acc_seeded staged table_stored out_staged out_stored
            conv_ready conv_act y_ready colsum out_centred out_squared sqsum gn_var gn_std gn_ready
            elu_arg elu_exp
            idx_staged rows_ready
            e_trans e_copied e_projected rows_added msg_ready onehot_ready c_agg c_acc
            dst_bc_free parts_ready parts_trans parts_copied far_ready hott_ready spread maxed step_t step_l
            rhs_ready shrink_log_ready max_kept expanded sc_t sc_l sc_d logit_ready weight_ready shrink_ready
            gat_onehot weighted g_agg g_acc0 g_acc1 dve_own pool_own pe_own act_own""".split()
        S = {n: sem(n) for n in names}
        slot_landed = [sem(f"slot_landed{i}") for i in range(RING)]
        edge_loaded = [sem(f"edge_loaded{i}") for i in range(UNROLL)]
        dst_bc_loaded = [sem(f"dst_bc_loaded{i}") for i in range(UNROLL)]

        block = ctx.enter_context(nc.Block())

        N_PARAMS = 2 + 7 + 1 + 2 + 8

        @block.sync
        def _(sp):
            sp.wait_ge(S["filled"], 1)
            groups2 = (GROUPS - 1 - HALF_G) * EG
            for g_tile, vecd in ((src_g, src), (dst_g, dst)):
                sp.dma_start(g_tile[:, 0, :], vecd[0:HALF_G * EG].rearrange("(g e) -> g e", e=EG)) \
                    .then_inc(S["edges_loaded"], 16)
                sp.dma_start(g_tile[0:HALF_G - 1, 1, :],
                             vecd[HALF_G * EG:HALF_G * EG + groups2].rearrange("(g e) -> g e", e=EG)) \
                    .then_inc(S["edges_loaded"], 16)
            sp.dma_start(src_g[HALF_G - 1:HALF_G, 1, :], src[LAST_EDGE:E].rearrange("(a e) -> a e", a=1)) \
                .then_inc(S["edges_loaded"], 16)
            sp.dma_start(dst_g[HALF_G - 1:HALF_G, 1, REPEATED:EG],
                         dst[LAST_EDGE + REPEATED:E].rearrange("(a e) -> a e", a=1)) \
                .then_inc(S["edges_loaded"], 16)
            sp.dma_start(x_sb[0:TAIL, WINDOWS - 1, :], x[(WINDOWS - 1) * P:N, :]).then_inc(S["x_loaded"], 16)
            sp.dma_start(x_sb[:, 0:WINDOWS - 1, :],
                         x[0:(WINDOWS - 1) * P, :].rearrange("(w p) f -> p w f", p=P)).then_inc(S["x_loaded"], 16)
            sp.wait_ge(S["dst16_ready"], 1)
            for b in range(2):
                sp.dma_start(dst_rows[b * HALF_G * EG:(b + 1) * HALF_G * EG].rearrange("(g e) -> g e", e=EG),
                             dst16_g[:, b, :]).then_inc(S["dst_rows_stored"], 16)

            def store_table(table, width, done):
                view = table.rearrange("(w p) f -> p w f", p=P)
                with sp.Fori(0, CHUNKS) as c:
                    sp.wait_ge(S["staged"], c + done + 1)
                    sp.dma_start(view[:, ds(c * CH, CH), :], width).then_inc(S["table_stored"], 16)

            store_table(conv_table, stage_conv, 0)
            sp.wait_ge(S["sched_ready"], 4)

            def load_edges(s, b, r):
                first = sp.value_load(first_edge[0:1, ds(s, 1)], min_val=0, max_val=LAST_EDGE)
                if past(s, UNROLL):
                    sp.wait_ge(S["e_trans"], s - (UNROLL - 1))
                sp.dma_start(edge_in[:, b, :],
                             edge_attr_128[ds(first, EG), :].rearrange("(p k) f -> p (k f)", k=K)) \
                    .then_inc(edge_loaded[b], 16)

            run_steps(sp, [(load_edges, 0)])
            for layer in range(2):
                store_table(gat_tables[layer], stage_gat, CHUNKS * (layer + 1))
                if layer == 0:
                    sp.wait_ge(S["dst_rows_stored"], 32)
                before = layer * STEPS

                def load_dst(s, b, r):
                    g = sp.value_load(sched[0:1, ds(s, 1)], min_val=0, max_val=GROUPS - 1)
                    if layer or past(s, UNROLL):
                        sp.wait_ge(S["far_ready"], before + s - (UNROLL - 1))
                    row = dst_rows[ds(g * EG, EG)].rearrange("(a e) -> a e", a=1)
                    sp.dma_start(dst_bc[:, b, :], row.to_broadcast([P, EG])).then_inc(dst_bc_loaded[b], 16)

                run_steps(sp, [(load_dst, 0)])
            view = out[0:(WINDOWS - 1) * P, :].rearrange("(w p) f -> p w f", p=P)
            with sp.Fori(0, CHUNKS - 1) as c:
                sp.wait_ge(S["out_staged"], c + 1)
                sp.dma_start(view[:, ds(c * CH, CH), :], x_sb[:, ds(c * CH, CH), :]).then_inc(S["out_stored"], 16)
            sp.wait_ge(S["out_staged"], CHUNKS)
            w0 = (CHUNKS - 1) * CH
            sp.dma_start(view[:, w0:WINDOWS - 1, :], x_sb[:, w0:WINDOWS - 1, :]).then_inc(S["out_stored"], 16)
            sp.dma_start(out[(WINDOWS - 1) * P:N, :], x_sb[0:TAIL, WINDOWS - 1, :]).then_inc(S["out_stored"], 16)
            sp.wait_ge(S["out_stored"], 16 * (CHUNKS + 1))

        @block.gpsimd
        def _(pool):
            own = Own(pool, S["pool_own"])
            pool.memset(x_sb[:, WINDOWS - 1, :], 0.0)
            pool.memset(head_w[:, :, :], 0.0)
            pool.memset(dst_g[:, 1, :], NOWHERE).then_inc(S["filled"], 1)
            pool.iota(iota_node[:, :], pattern=[[1, WINDOWS * P]], base=0, channel_multiplier=0)
            pool.iota(step128, pattern=[[P, STEPS]], base=0, channel_multiplier=0,
                      allow_small_or_imprecise_dtypes=True)
            pool.iota(reach[:, 2:4], pattern=[[P * HALF_G, 2]], base=0, channel_multiplier=P,
                      allow_small_or_imprecise_dtypes=True)
            pool.iota(far_node[:, :], pattern=[[P, WINDOWS]], base=0, channel_multiplier=1,
                      allow_small_or_imprecise_dtypes=True).then_inc(S["ids_ready"], 1)
            pool.memset(ident[:, :], 0.0)
            pool.memset(ones[:, :], 1.0)
            pool.memset(one_col[:, :], 1.0)
            own(pool.memset(pick[:, :, :], 1.0))
            own(pool.affine_select(out=ident[:, :], in_=ident[:, :], compare_op=ALU.not_equal, fill=1.0, base=0,
                                   pattern=[[-1, P]], channel_multiplier=1))
            pool.tensor_copy(ident_bf[:, :], ident[:, :])
            pool.affine_select(out=ones_tail[:, :], in_=ones[:, :], compare_op=ALU.is_gt, fill=0.0, base=TAIL,
                               pattern=[[0, P]], channel_multiplier=-1)
            own(pool.affine_select(out=pick[:, :, :], in_=pick[:, :, :], compare_op=ALU.is_ge, fill=0.0, base=0,
                                   pattern=[[-3, K * HEADS], [0, P]], channel_multiplier=1))
            pool.affine_select(out=pick[:, :, :], in_=pick[:, :, :], compare_op=ALU.is_ge, fill=0.0, base=2,
                               pattern=[[3, K * HEADS], [0, P]], channel_multiplier=-1).then_inc(S["consts"], 1)
            pool.wait_ge(S["idx_ready"], 1)
            pool.wait_ge(S["sched_ready"], 4)

            def gather_group(layer, table, width, used, i, slot, first_round):
                half, j = slot // HALF_R, slot % HALF_R
                if j == 0:
                    pool.tensor_copy(idx_stage[:, half, :],
                                     src_idx[:, ds(i * (RING * K) + half * HALF_R * K, HALF_R * K)]) \
                        .then_inc(S["idx_staged"], 1)
                    pool.wait_ge(S["idx_staged"], (i + layer * ROUNDS) * 2 + half + 1)
                if not first_round:
                    steps = pool.value_load(freed_at[0:1, ds(i * RING + (slot - RING), 1)], min_val=1, max_val=STEPS)
                    pool.wait_ge(used[0], steps + used[1])
                if slot >= IN_FLIGHT or not first_round:
                    before = slot - IN_FLIGHT
                    back = before < 0
                    pool.wait_ge(slot_landed[before % RING], (i + (layer * ROUNDS + (0 if back else 1))) * (16 * K))
                    pool.sem_inc(S["rows_ready"], 1)
                for k in range(K):
                    pool.indirect_dma_start(
                        out=rows[:, slot, k, 0:width], out_offset=None, in_=table,
                        in_offset=bass.IndirectOffsetOnAxis(ap=idx_stage[:, half, j * K + k:j * K + k + 1], axis=0)) \
                        .then_inc(slot_landed[slot], 16)

            for layer, (table, width, used) in enumerate([
                    (conv_table, D, (S["rows_added"], 0)),
                    (gat_tables[0], ROW, (S["weighted"], 0)),
                    (gat_tables[1], ROW, (S["weighted"], STEPS))]):
                pool.wait_ge(S["table_stored"], 16 * CHUNKS * (layer + 1))
                if layer:
                    pool.wait_ge(S["acc_seeded"], CHUNKS * layer)
                for slot in range(RING):
                    gather_group(layer, table, width, used, 0, slot, True)
                with pool.Fori(1, ROUNDS) as i:
                    for slot in range(RING):
                        gather_group(layer, table, width, used, i, slot, False)
                for slot in range(RING - IN_FLIGHT, RING):
                    pool.wait_ge(slot_landed[slot], (layer + 1) * ROUNDS * 16 * K)
                    pool.sem_inc(S["rows_ready"], 1)

        @block.scalar
        def _(act):
            own = Own(act, S["act_own"])
            act.dma_start(w_raw[:, 0, :], L0_gnn_w1).then_inc(S["params_loaded"], 16)
            act.dma_start(w_raw[:, 1, :], L0_gnn_we).then_inc(S["params_loaded"], 16)
            for i, v in enumerate((L0_gnn_b1, L0_gnn_be, L0_gnn_gn_weight, L0_gnn_gn_bias, L0_gnn_gn_mean_scale,
                                   L1_gnn_b1, L1_gnn_b2)):
                act.dma_start(vec[:, i, :], v.rearrange("(a f) -> a f", a=1).to_broadcast([P, D])) \
                    .then_inc(S["params_loaded"], 16)
            act.dma_start(one_eps[:, :], L0_gnn_eps.to_broadcast([P, 1])).then_inc(S["params_loaded"], 16)
            act.dma_start(aug[:, 0, 0:D], L1_gnn_W1).then_inc(S["params_loaded"], 16)
            act.dma_start(aug[:, 1, 0:D], L1_gnn_W2).then_inc(S["params_loaded"], 16)
            act.wait_ge(S["filled"], 1)
            for n, (a_src, a_dst) in enumerate(((L1_gnn_a_src1, L1_gnn_a_dst1), (L1_gnn_a_src2, L1_gnn_a_dst2))):
                for i, a in enumerate((a_src, a_dst)):
                    for h in range(HEADS):
                        act.dma_start(head_w[h * HID:(h + 1) * HID, n, i * HEADS + h:i * HEADS + h + 1],
                                      a[h:h + 1, :].rearrange("a f -> f a")).then_inc(S["params_loaded"], 16)

            act.wait_ge(S["w_trans"], 1)
            act.activation(w1_t[:, :], bank[0][:, 0:D], ACT.Copy)
            act.activation(we_t[:, :], bank[0][:, D:2 * D], ACT.Copy)
            act.activation(w2_t[:, :, :], bank[0][:, 2 * D:4 * D].rearrange("p (a f) -> p a f", a=2), ACT.Copy) \
                .then_inc(S["w_trans_copied"], 1)

            def norm(c, done, keep):
                act.wait_ge(S["centred"], c + done + 1)
                act.activation(T2, T1, ACT.Square).then_inc(S["squared"], 1)
                act.wait_ge(S["variance"], c + done + 1)
                act.activation(stats[:, 4, :], stats[:, 3, :], ACT.Sqrt).then_inc(S["std"], 1)
                act.wait_ge(S["scaled"], c + done + 1)
                if keep:
                    act.activation(h_sb[:, ds(c * CH, CH), :], T1, ACT.Relu)
                act.activation(FEAT, T1, ACT.Relu).then_inc(S["feat_ready"], 1)

            def copy_feat(c, done):
                act.wait_ge(S["feat_trans"], c + done + 1)
                act.activation(FEAT_T[:, 0:4, :], bank[0][:, :].rearrange("p (w c) -> p w c", c=D), ACT.Copy)
                act.activation(FEAT_T[:, 4:CH, :], bank[1][:, 0:3 * D].rearrange("p (w c) -> p w c", c=D),
                               ACT.Copy).then_inc(S["feat_copied"], 1)

            def seed_acc(c, done):
                act.wait_ge(S["evacuated"], c + done + 1)
                act.activation(acc_heads[:, ds(c * CH, CH), :, 0:HID],
                               stage_gat[:, :, 0:D].rearrange("p t (h c) -> p t h c", h=HEADS), ACT.Copy) \
                    .then_inc(S["acc_seeded"], 1)

            with act.Fori(0, CHUNKS) as c:
                norm(c, 0, True)
                copy_feat(c, 0)

            def copy_edge(s, b, r):
                act.wait_ge(S["e_trans"], s + 1)
                if past(s, 2):
                    act.wait_ge(S["e_projected"], s - 1)
                act.activation(edge_t[:, b % 2, :], trans_ps[b % 2][:, :], ACT.Copy).then_inc(S["e_copied"], 1)

            def silu(s, b, r):
                act.wait_ge(S["rows_added"], s + 1)
                if past(s, UNROLL):
                    act.wait_ge(S["c_agg"], s - (UNROLL - 1))
                act.activation(msg[:, b, :, 0:D], pre_act[:, b % 2, :].rearrange("p (k f) -> p k f", k=K), ACT.Silu) \
                    .then_inc(S["msg_ready"], 1)

            run_steps(act, [(copy_edge, 0), (silu, 2)])

            with act.Fori(0, CHUNKS) as c:
                act.wait_ge(S["conv_ready"], c + 1)
                act.activation(acc[:, ds(c * CH, CH), 0:D], hw_sb[:, ds(c * CH, CH), :], ACT.Silu) \
                    .then_inc(S["conv_act"], 1)
            with act.Fori(0, CHUNKS) as c:
                act.wait_ge(S["out_centred"], c + 1)
                act.wait_ge(S["sqsum"], c)
                act.activation(T2, T1, ACT.Square).then_inc(S["out_squared"], 1)
            act.wait_ge(S["gn_var"], 1)
            act.activation(cvec[:, 3, :], cvec[:, 2, :], ACT.Sqrt).then_inc(S["gn_std"], 1)
            with act.Fori(0, CHUNKS) as c:
                norm(c, CHUNKS, False)
                copy_feat(c, CHUNKS)
                seed_acc(c, CHUNKS)

            for layer in range(2):
                before = layer * STEPS

                def stage_parts_(s, b, r):
                    g = act.value_load(sched[0:1, ds(s, 1)], min_val=0, max_val=GROUPS - 1)
                    act.wait_ge(S["rows_ready"], g + ((layer + 1) * GROUPS + 1))
                    if layer or past(s, 2):
                        act.wait_ge(S["parts_trans"], before + s - 1)
                    slot = act.snap(g % RING, min_val=0, max_val=RING - 1)
                    ring = rows[:, :, :, :].bitcast(BF16)[:, ds(slot, 1), :, 2 * (D + HEADS):2 * ROW] \
                        .rearrange("p a k c -> p (a k) c")
                    act.activation(parts[:, b % 2, :].rearrange("p (k c) -> p k c", k=K), ring, ACT.Copy) \
                        .then_inc(S["parts_ready"], 1)

                def far_mask(s, b, r):
                    w = act.value_load(window_of[0:1, ds(s, 1)], min_val=0, max_val=WINDOWS - 1)
                    act.wait_ge(dst_bc_loaded[b], (r + layer * (STEPS // UNROLL) + 1) * 16)
                    if layer or past(s, 2):
                        act.wait_ge(S["maxed"], before + s - 1)
                    act.activation(far[:, b % 2, :].rearrange("n (k p) -> n k p", k=K),
                                   dst_bc[:, b, :].rearrange("n (p k) -> n k p", k=K), ACT.Abs,
                                   bias=far_node[:, ds(w, 1)], scale=FAR).then_inc(S["far_ready"], 1)

                def one_hot_t(s, b, r):
                    act.wait_ge(S["far_ready"], before + s + 1)
                    if layer or past(s, UNROLL):
                        act.wait_ge(S["expanded"], before + s - (UNROLL - 1))
                    act.activation(onehot_t[:, b, :], far[:, b % 2, :], ACT.Relu, bias=one_col[:, :], scale=-1.0) \
                        .then_inc(S["hott_ready"], 1)

                def copy_parts(s, b, r):
                    act.wait_ge(S["parts_trans"], before + s + 1)
                    if layer or past(s, 2):
                        act.wait_ge(S["spread"], before + s - 1)
                    act.activation(parts_t[:, b % 2, :], bank_bf[0:K * HEADS * 3, 0:P], ACT.Copy) \
                        .then_inc(S["parts_copied"], 1)

                def exponentials(s, b, r):
                    act.wait_ge(S["logit_ready"], before + s + 1)
                    if layer or past(s, UNROLL):
                        act.wait_ge(S["g_agg"], before + s - (UNROLL - 1))
                    act.activation(msg_heads[:, b, :, :, HID],
                                   logit[:, b, :].rearrange("p (k h) -> p k h", k=K), ACT.Exp) \
                        .then_inc(S["weight_ready"], 1)
                    if layer or past(s, UNROLL):
                        act.wait_ge(S["g_acc1"], before + s - (UNROLL - 1))
                    act.activation(shrink[:, b, :], shrink_log[:, b, :], ACT.Exp).then_inc(S["shrink_ready"], 1)

                run_steps(act, [(copy_parts, 1), (stage_parts_, 0), (far_mask, 0), (one_hot_t, 0), (exponentials, 3)])

                with act.Fori(0, CHUNKS) as c:
                    act.wait_ge(S["elu_arg"], c + layer * CHUNKS + 1)
                    act.activation(T2, T2, ACT.Exp).then_inc(S["elu_exp"], 1)
                    if layer == 0:
                        copy_feat(c, 2 * CHUNKS)
                        seed_acc(c, 2 * CHUNKS)

        @block.tensor
        def _(pe):
            pe.wait_ge(S["consts"], 1)
            pe.wait_ge(S["edgef_ready"], 2)
            for i, g_tile in enumerate((srcf_g, dstf_g)):
                for b in range(2):
                    for k in range(K):
                        last = pe.transpose(bank[2 * i + b][:, k * HALF_G:(k + 1) * HALF_G],
                                            g_tile[:, b, k::K], ident[0:HALF_G, 0:HALF_G])
            last.then_inc(S["edge_t_ready"], 1)
            pe.wait_ge(S["past_ready"], 1)
            pe.matmul(bank[4][0:1, 0:STEPS], ones[0:HALF_G, 0:1], past_g[:, 0, :], start=True, stop=False)
            pe.matmul(bank[4][0:1, 0:STEPS], ones[0:HALF_G - 1, 0:1], past_g[0:HALF_G - 1, 1, :],
                      start=False, stop=True)
            for b in range(2):
                last = pe.matmul(bank[5][0:1, b * HALF_G:(b + 1) * HALF_G], reach[:, 6 + b:7 + b],
                                 ident[0:HALF_G, 0:HALF_G], start=True, stop=True)
            last.then_inc(S["sched_ps"], 1)
            pe.wait_ge(S["params_loaded"], 16 * N_PARAMS)
            pe.wait_ge(S["idx_ready"], 1)
            for i, w in enumerate((w_raw[:, 0, :], w_raw[:, 1, :], aug[:, 0, 0:D], aug[:, 1, 0:D])):
                last = pe.transpose(bank[0][:, i * D:(i + 1) * D], w, ident[:, :])
            last.then_inc(S["w_trans"], 1)
            pe.wait_ge(S["w_trans_copied"], 1)
            for n in range(2):
                last = pe.matmul(bank[1][:, n * 2 * HEADS:(n + 1) * 2 * HEADS], w2_t[:, n, :], head_w[:, n, :],
                                 start=True, stop=True)
            last.then_inc(S["aug_ps"], 1)
            pe.wait_ge(S["aug_ready"], 1)

            def project(c, done, weight, width):
                pe.wait_ge(S["feat_ready"], c + done + 1)
                if done:
                    pe.wait_ge(S["feat_copied"], c + done)
                for j in range(CH):
                    last = pe.transpose(bank[j // 4][:, (j % 4) * D:(j % 4 + 1) * D], FEAT[:, j, :], ident[:, :])
                last.then_inc(S["feat_trans"], 1)
                pe.wait_ge(S["feat_copied"], c + done + 1)
                pe.wait_ge(S["evacuated"], c + done)
                for j in range(CH):
                    last = pe.matmul(proj(j, 1, slice(0, width)).rearrange("p a c -> p (a c)")
                                     if j % 3 == 0 else
                                     bank[2 + j // 3][:, (j % 3) * SLOT:(j % 3) * SLOT + width],
                                     FEAT_T[:, j, :], weight, start=True, stop=True)
                last.then_inc(S["projected"], 1)

            with pe.Fori(0, CHUNKS) as c:
                project(c, 0, w1_t[:, :], D)

            def transpose_edges(s, b, r):
                pe.wait_ge(edge_loaded[b], (r + 1) * 16)
                if past(s, 2):
                    pe.wait_ge(S["e_copied"], s - 1)
                for k in range(K):
                    last = pe.transpose(trans_ps[b % 2][:, k * P:(k + 1) * P], edge_in[:, b, k * P:(k + 1) * P],
                                        ident[:, :])
                last.then_inc(S["e_trans"], 1)

            def project_edges(s, b, r):
                pe.wait_ge(S["e_copied"], s + 1)
                if past(s, 2):
                    pe.wait_ge(S["rows_added"], s - 1)
                for k in range(K):
                    last = pe.matmul(edge_ps[b % 2][:, k * P:(k + 1) * P], edge_t[:, b % 2, k * P:(k + 1) * P],
                                     we_t[:, :], start=True, stop=True)
                last.then_inc(S["e_projected"], 1)

            def aggregate(s, b, r):
                pe.wait_ge(S["msg_ready"], s + 1)
                pe.wait_ge(S["onehot_ready"], s + 1)
                if past(s, 2):
                    pe.wait_ge(S["c_acc"], s - 1)
                for k in range(K):
                    last = pe.matmul(agg_ps[b % 2][:, 0:D], onehot[:, b, k, :], msg[:, b, k, 0:D],
                                     start=(k == 0), stop=(k == K - 1))
                last.then_inc(S["c_agg"], 1)

            run_steps(pe, [(aggregate, 3), (project_edges, 1), (transpose_edges, 0)])

            def column_sums(tiles, ready, done, value):
                def chunk(c, first, last_):
                    pe.wait_ge(ready, c + 1)
                    t = tiles(c)
                    pe.matmul(bank[0][:, :], ones[:, :], t[:, 0:4, :], start=first, stop=last_)
                    pe.matmul(bank[1][:, 0:2 * D], ones[:, :], t[:, 4:6, :], start=first, stop=last_)
                    return pe.matmul(bank[2][:, 0:D], (ones_tail if last_ else ones)[:, :], t[:, 6:CH, :],
                                     start=first, stop=last_)
                chunk(0, True, False).then_inc(done, 1)
                with pe.Fori(1, CHUNKS - 1) as c:
                    chunk(c, False, False).then_inc(done, 1)
                chunk(CHUNKS - 1, False, True).then_inc(done, 1)

            column_sums(lambda c: acc[:, ds(c * CH, CH), 0:D], S["y_ready"], S["colsum"], 0)
            pe.wait_ge(S["out_centred"], 1)
            column_sums(lambda c: T2, S["out_squared"], S["sqsum"], 0)

            for layer in range(2):
                with pe.Fori(0, CHUNKS) as c:
                    project(c, CHUNKS * (layer + 1), aug[:, layer, :], AUG)
                before = layer * STEPS

                def transpose_parts(s, b, r):
                    pe.wait_ge(S["parts_ready"], before + s + 1)
                    if layer or past(s, 1):
                        pe.wait_ge(S["parts_copied"], before + s)
                    pe.transpose(bank_bf[0:K * HEADS * 3, 0:P], parts[:, b % 2, :], ident_bf[:, :]) \
                        .then_inc(S["parts_trans"], 1)

                def spread_scores(s, b, r):
                    pe.wait_ge(S["parts_copied"], before + s + 1)
                    if layer or past(s, 2):
                        pe.wait_ge(S["maxed"], before + s - 1)
                    for k in range(K):
                        for h in range(HEADS):
                            last = pe.matmul(score_ps[b % 2][h][:, k * P:(k + 1) * P], pick[:, k * HEADS + h, :],
                                             parts_t[:, b % 2, :], start=True, stop=True)
                    last.then_inc(S["spread"], 1)

                def expand(s, b, r):
                    pe.wait_ge(S["hott_ready"], before + s + 1)
                    pe.wait_ge(S["rhs_ready"], before + s + 1)
                    if layer or past(s, 1):
                        pe.wait_ge(S["sc_d"], before + s)
                    for k in range(K):
                        at = k * 2 * HEADS
                        last = pe.matmul(exp_ps[:, at:at + 2 * HEADS], onehot_t[:, b, k * P:(k + 1) * P],
                                         step_rhs[:, b, :], start=True, stop=True)
                    last.then_inc(S["expanded"], 1)

                def sum_messages(s, b, r):
                    pe.wait_ge(S["weighted"], before + s + 1)
                    pe.wait_ge(S["gat_onehot"], before + s + 1)
                    if layer or past(s, 2):
                        pe.wait_ge(S["g_acc1"], before + s - 1)
                    for k in range(K):
                        last = pe.matmul(agg_ps[b % 2][:, 0:HEADS * (HID + 1)], onehot[:, b, k, :], msg[:, b, k, :],
                                         start=(k == 0), stop=(k == K - 1))
                    last.then_inc(S["g_agg"], 1)

                pe.wait_ge(S["evacuated"], CHUNKS * (layer + 2))
                run_steps(pe, [(sum_messages, 5), (spread_scores, 1), (expand, 2), (transpose_parts, 0)])

        @block.vector
        def _(dve):
            own = Own(dve, S["dve_own"])
            V = nc.vector
            dve.wait_ge(S["edges_loaded"], 16 * 6)
            dve.wait_ge(S["filled"], 1)
            V.tensor_copy(srcf_g, src_g).then_inc(S["edgef_ready"], 1)
            V.tensor_copy(dstf_g, dst_g).then_inc(S["edgef_ready"], 1)
            V.tensor_copy(dst16_g, dst_g).then_inc(S["dst16_ready"], 1)
            dve.wait_ge(S["ids_ready"], 1)
            dve.wait_ge(S["edgef_ready"], 2)
            own(V.tensor_tensor(reach[:, 0:2], dstf_g[:, :, EG - 1], reach[:, 2:4], ALU.add))
            for b in range(2):
                ins = V.tensor_scalar(past_g[:, b, :], step128, reach[:, b:b + 1], None, ALU.is_gt)
            own(ins)
            own(V.tensor_reduce(reach[:, 4:6], past_g, AX.X, ALU.add))
            V.tensor_scalar(reach[:, 6:8], reach[:, 4:6], -1.0, float(STEPS), ALU.mult, ALU.add) \
                .then_inc(S["past_ready"], 1)
            V.tensor_scalar(far_node[:, :], far_node[:, :], -FAR, None, ALU.mult)
            dve.wait_ge(S["edge_t_ready"], 1)
            for i, to in enumerate((src_idx, dst_col)):
                for b in range(2):
                    ins = V.tensor_copy(
                        to[:, b * HALF_G * K:(b + 1) * HALF_G * K].rearrange("p (g k) -> p k g", k=K),
                        bank[2 * i + b][:, 0:K * HALF_G].rearrange("p (k g) -> p k g", k=K))
            ins.then_inc(S["idx_ready"], 1)
            dve.wait_ge(S["sched_ps"], 1)
            V.tensor_copy(sched[:, :], bank[4][0:1, 0:STEPS]).then_inc(S["sched_ready"], 1)
            V.scalar_tensor_tensor(out=window_of[:, :], in0=step128[0:1, :], scalar=1.0 / P, in1=bank[4][0:1, 0:STEPS],
                                   op0=ALU.mult, op1=ALU.subtract).then_inc(S["sched_ready"], 1)
            V.tensor_scalar(first_edge[:, :], bank[4][0:1, 0:STEPS], float(EG), float(LAST_EDGE), ALU.mult, ALU.min) \
                .then_inc(S["sched_ready"], 1)
            V.tensor_copy(freed_at[:, :], bank[5][0:1, 0:GROUPS]).then_inc(S["sched_ready"], 1)
            dve.wait_ge(S["params_loaded"], 16 * N_PARAMS)
            V.tensor_tensor(cvec[:, 5, :], vec[:, B1, :], vec[:, BE, :], ALU.add)
            V.tensor_scalar(one_eps[:, :], one_eps[:, :], 1.0, None, ALU.add)
            dve.wait_ge(S["aug_ps"], 1)
            own(V.tensor_copy(aug[:, :, D:AUG], bank[1][:, 0:4 * HEADS].rearrange("p (n c) -> p n c", n=2)))
            V.sem_inc(S["aug_ready"], 1)
            dve.wait_ge(S["sched_ready"], 4)
            dve.wait_ge(S["dst_rows_stored"], 32)
            own(V.memset(acc[:, :, :], 0.0))

            def all_windows(v):
                return v[:, None, :].to_broadcast([P, CH, D])

            def per_window(v):
                return v[:, :, None].to_broadcast([P, CH, D])

            def norm(c, done, source):
                V.sem_inc(S["norm_begun"], 1)
                own(V.tensor_reduce(stats[:, 0, :], source, AX.X, ALU.add))
                own(V.tensor_scalar(stats[:, 1, :], stats[:, 0, :], -1.0 / D, None, ALU.mult))
                V.tensor_tensor(T1, source, per_window(stats[:, 1, :]), ALU.add).then_inc(S["centred"], 1)
                dve.wait_ge(S["squared"], c + done + 1)
                own(V.tensor_reduce(stats[:, 2, :], T2, AX.X, ALU.add))
                V.tensor_scalar(stats[:, 3, :], stats[:, 2, :], 1.0 / D, LN_EPS, ALU.mult, ALU.add) \
                    .then_inc(S["variance"], 1)
                dve.wait_ge(S["std"], c + done + 1)
                own(V.reciprocal(stats[:, 5, :], stats[:, 4, :]))
                V.tensor_tensor(T1, T1, per_window(stats[:, 5, :]), ALU.mult).then_inc(S["scaled"], 1)
            NORM_OWN = 4

            def stage_rows(c, done):
                dve.wait_ge(S["projected"], c + done + 1)
                dve.wait_ge(S["table_stored"], (c + done) * 16)
                dve.wait_ge(S["acc_seeded"], c + done - CHUNKS)
                for j, n in PROJ:
                    V.tensor_copy(node_scores[:, ds(c * CH + j, n), 0:HEADS], proj(j, n, slice(D + HEADS, AUG)))
                    ins = V.tensor_copy(stage_gat[:, j:j + n, 0:D + HEADS], proj(j, n, slice(0, D + HEADS)))
                own(ins)
                V.sem_inc(S["evacuated"], 1)
                own_score = stage_gat[:, :, D:D + HEADS]
                part = [stage_parts[:, :, :, i] for i in range(3)]
                state = node_scores[:, ds(c * CH, CH), :]
                own(V.tensor_copy(part[0], own_score))
                own(V.tensor_tensor(gat_tmp[:, 0, :, :], own_score, part[0], ALU.subtract))
                own(V.tensor_copy(part[1], gat_tmp[:, 0, :, :]))
                own(V.tensor_tensor(part[2], gat_tmp[:, 0, :, :], part[1], ALU.subtract))
                own(V.tensor_tensor(gat_tmp[:, 1, :, :], own_score, state[:, :, 0:HEADS], ALU.add))
                V.sem_inc(S["staged"], 1)
                V.scalar_tensor_tensor(out=state[:, :, HEADS:2 * HEADS], in0=gat_tmp[:, 1, :, :], scalar=SLOPE,
                                       in1=gat_tmp[:, 1, :, :], op0=ALU.mult, op1=ALU.max)
                own(V.tensor_copy(acc_heads[:, ds(c * CH, CH), :, HID],
                                  ones[:, 0:CH * HEADS].rearrange("p (w h) -> p w h", h=HEADS)))
            STAGE_OWN = 7

            dve.wait_ge(S["x_loaded"], 32)
            with own.loop(0, CHUNKS, NORM_OWN + 1) as c:
                norm(c, 0, x_sb[:, ds(c * CH, CH), :])
                dve.wait_ge(S["projected"], c + 1)
                dve.wait_ge(S["table_stored"], c * 16)
                for j, n in PROJ:
                    V.tensor_tensor(hw_sb[:, ds(c * CH + j, n), :], proj(j, n, slice(0, D)),
                                    vec[:, B1:B1 + 1, :].to_broadcast([P, n, D]), ALU.add)
                    ins = V.tensor_tensor(stage_conv[:, j:j + n, :], proj(j, n, slice(0, D)),
                                          cvec[:, 5:6, :].to_broadcast([P, n, D]), ALU.add)
                own(ins)
                V.sem_inc(S["evacuated"], 1)
                V.sem_inc(S["staged"], 1)

            def group_at(s):
                return dve.value_load(sched[0:1, ds(s, 1)], min_val=0, max_val=GROUPS - 1)

            def window_at(s):
                return dve.value_load(window_of[0:1, ds(s, 1)], min_val=0, max_val=WINDOWS - 1)

            def one_hot(s, b, free, ready, free_count, base):
                g, w = group_at(s), window_at(s)
                if free_count is not None:
                    dve.wait_ge(free, free_count)
                V.tensor_tensor(onehot[:, b, :, :],
                                iota_node[:, ds(w * P, P)][:, None, :].to_broadcast([P, K, P]),
                                dst_col[:, ds(g * K, K)][:, :, None].to_broadcast([P, K, P]), ALU.is_equal) \
                    .then_inc(ready, 1)

            def add_rows(s, b, r):
                g = group_at(s)
                slot = dve.snap(g % RING, min_val=0, max_val=RING - 1)
                dve.wait_ge(S["rows_ready"], g + 1)
                dve.wait_ge(S["e_projected"], s + 1)
                if past(s, 2):
                    dve.wait_ge(S["msg_ready"], s - 1)
                V.tensor_tensor(pre_act[:, b % 2, :].rearrange("p (k f) -> p k f", k=K),
                                edge_ps[b % 2][:, :].rearrange("p (k f) -> p k f", k=K),
                                rows[:, ds(slot, 1), :, 0:D].rearrange("p a k f -> p (a k) f"), ALU.add) \
                    .then_inc(S["rows_added"], 1)

            def conv_one_hot(s, b, r):
                one_hot(s, b, S["c_agg"], S["onehot_ready"], s - (UNROLL - 1) if past(s, UNROLL) else None, 0)

            def add_sums(s, b, r):
                w = window_at(s)
                dve.wait_ge(S["c_agg"], s + 1)
                if past(s, 1):
                    dve.wait_ge(S["c_acc"], s)
                to = acc[:, ds(w, 1), 0:D].rearrange("p a f -> p (a f)")
                V.tensor_tensor(to, to, agg_ps[b % 2][:, 0:D], ALU.add).then_inc(S["c_acc"], 1)

            run_steps(dve, [(conv_one_hot, 1), (add_rows, 1), (add_sums, 4)])

            dve.wait_ge(S["c_acc"], STEPS)
            with dve.Fori(0, CHUNKS) as c:
                at = ds(c * CH, CH)
                V.scalar_tensor_tensor(out=hw_sb[:, at, :], in0=hw_sb[:, at, :], scalar=one_eps[:, 0:1],
                                       in1=acc[:, at, 0:D], op0=ALU.mult, op1=ALU.add).then_inc(S["conv_ready"], 1)
            with dve.Fori(0, CHUNKS) as c:
                at = ds(c * CH, CH)
                dve.wait_ge(S["conv_act"], c + 1)
                V.tensor_tensor(acc[:, at, 0:D], acc[:, at, 0:D], h_sb[:, at, :], ALU.add).then_inc(S["y_ready"], 1)

            def add_windows(to):
                own(V.tensor_reduce(cvec[:, 0, :], bank[0][:, :].rearrange("p (w f) -> p f w", f=D), AX.X, ALU.add))
                own(V.tensor_reduce(cvec[:, 1, :], bank[1][:, 0:2 * D].rearrange("p (w f) -> p f w", f=D), AX.X, ALU.add))
                own(V.tensor_tensor(to, cvec[:, 0, :], cvec[:, 1, :], ALU.add))
                own(V.tensor_tensor(to, to, bank[2][:, 0:D], ALU.add))

            dve.wait_ge(S["colsum"], CHUNKS)
            add_windows(cvec[:, 2, :])
            own(V.scalar_tensor_tensor(out=cvec[:, 4, :], in0=cvec[:, 2, :], scalar=1.0 / max(N, 1),
                                       in1=vec[:, GNMS, :], op0=ALU.mult, op1=ALU.mult))
            with dve.Fori(0, CHUNKS) as c:
                dve.wait_ge(S["out_squared"], c)
                V.tensor_tensor(T1, acc[:, ds(c * CH, CH), 0:D], all_windows(cvec[:, 4, :]), ALU.subtract) \
                    .then_inc(S["out_centred"], 1)
            dve.wait_ge(S["sqsum"], CHUNKS)
            add_windows(cvec[:, 2, :])
            own(V.tensor_scalar(cvec[:, 2, :], cvec[:, 2, :], 1.0 / max(N, 1), GN_EPS, ALU.mult, ALU.add))
            V.sem_inc(S["gn_var"], 1)
            dve.wait_ge(S["gn_std"], 1)
            own(V.reciprocal(cvec[:, 0, :], cvec[:, 3, :]))
            own(V.tensor_tensor(cvec[:, 1, :], cvec[:, 0, :], vec[:, GNW, :], ALU.mult))
            own(V.tensor_tensor(cvec[:, 4, :], cvec[:, 4, :], cvec[:, 1, :], ALU.mult))
            own(V.tensor_tensor(cvec[:, 4, :], vec[:, GNB, :], cvec[:, 4, :], ALU.subtract))
            with own.loop(0, CHUNKS, 3 + NORM_OWN + STAGE_OWN) as c:
                at = ds(c * CH, CH)
                own(V.tensor_tensor(T1, acc[:, at, 0:D], all_windows(cvec[:, 1, :]), ALU.mult))
                own(V.tensor_tensor(x_sb[:, at, :], x_sb[:, at, :], T1, ALU.add))
                own(V.tensor_tensor(x_sb[:, at, :], x_sb[:, at, :], all_windows(cvec[:, 4, :]), ALU.add))
                norm(c, CHUNKS, x_sb[:, at, :])
                stage_rows(c, CHUNKS)
            for layer in range(2):
                before = layer * STEPS

                def window_max(s, b, r):
                    w = window_at(s)
                    state = node_scores[:, ds(w, 1), :].rearrange("p a c -> p (a c)")
                    if isinstance(s, int) and s == 0:
                        dve.wait_ge(S["acc_seeded"], CHUNKS * (layer + 1))
                    if layer or past(s, 1):
                        dve.wait_ge(S["max_kept"], before + s)
                    if layer or past(s, UNROLL):
                        dve.wait_ge(S["expanded"], before + s - (UNROLL - 1))
                    dve.wait_ge(S["spread"], before + s + 1)
                    dve.wait_ge(S["far_ready"], before + s + 1)
                    if layer or past(s, 1):
                        dve.wait_ge(S["maxed"], before + s)
                    V.tensor_copy(step_rhs[:, b, 0:HEADS], state[:, 0:HEADS])
                    for h in range(HEADS):
                        ins = V.tensor_tensor_reduce(out=masked[:, h, :], in0=score_ps[b % 2][h][:, :],
                                                     in1=far[:, b % 2, :], scale=1.0, scalar=-3.0e38,
                                                     op0=ALU.subtract, op1=ALU.max,
                                                     accum_out=local_max[:, b % 2, h:h + 1])
                    ins.then_inc(S["maxed"], 1)
                    dve.wait_ge(S["maxed"], before + s + 1)
                    V.tensor_tensor(tmp_m[:, b % 2, 0, :], local_max[:, b % 2, :], state[:, 0:HEADS], ALU.add) \
                        .then_inc(S["step_t"], 1)
                    dve.wait_ge(S["step_t"], before + s + 1)
                    V.scalar_tensor_tensor(out=tmp_m[:, b % 2, 1, :], in0=tmp_m[:, b % 2, 0, :], scalar=SLOPE,
                                           in1=tmp_m[:, b % 2, 0, :], op0=ALU.mult, op1=ALU.max) \
                        .then_inc(S["step_l"], 1)
                    dve.wait_ge(S["step_l"], before + s + 1)
                    V.tensor_tensor(step_rhs[:, b, HEADS:2 * HEADS], tmp_m[:, b % 2, 1, :], state[:, HEADS:2 * HEADS],
                                    ALU.max).then_inc(S["rhs_ready"], 1)
                    dve.wait_ge(S["rhs_ready"], before + s + 1)
                    if layer or past(s, UNROLL):
                        dve.wait_ge(S["shrink_ready"], before + s - (UNROLL - 1))
                    V.tensor_tensor(shrink_log[:, b, :], state[:, HEADS:2 * HEADS], step_rhs[:, b, HEADS:2 * HEADS],
                                    ALU.subtract).then_inc(S["shrink_log_ready"], 1)
                    dve.wait_ge(S["shrink_log_ready"], before + s + 1)
                    V.tensor_scalar(state[:, HEADS:2 * HEADS], step_rhs[:, b, HEADS:2 * HEADS], 1.0, None, ALU.mult) \
                        .then_inc(S["max_kept"], 1)

                def logits(s, b, r):
                    g = group_at(s)
                    slot = dve.snap(g % RING, min_val=0, max_val=RING - 1)
                    dve.wait_ge(S["expanded"], before + s + 1)
                    dve.wait_ge(S["rows_ready"], g + ((layer + 1) * GROUPS + 1))
                    both = exp_ps[:, 0:K * 2 * HEADS].rearrange("p (k c) -> p k c", k=K)
                    t = [score[:, b % 2, i, :].rearrange("p (k h) -> p k h", k=K) for i in range(3)]
                    V.tensor_tensor(t[0], both[:, :, 0:HEADS],
                                    rows[:, ds(slot, 1), :, D:D + HEADS].rearrange("p a k f -> p (a k) f"), ALU.add) \
                        .then_inc(S["sc_t"], 1)
                    dve.wait_ge(S["sc_t"], before + s + 1)
                    V.scalar_tensor_tensor(out=t[1], in0=t[0], scalar=SLOPE, in1=t[0], op0=ALU.mult, op1=ALU.max) \
                        .then_inc(S["sc_l"], 1)
                    dve.wait_ge(S["sc_l"], before + s + 1)
                    V.tensor_tensor(t[2], t[1], both[:, :, HEADS:2 * HEADS], ALU.subtract).then_inc(S["sc_d"], 1)
                    dve.wait_ge(S["sc_d"], before + s + 1)
                    if layer or past(s, UNROLL):
                        dve.wait_ge(S["weight_ready"], before + s - (UNROLL - 1))
                    V.tensor_scalar(logit[:, b, :], score[:, b % 2, 2, :], 0.0, None, ALU.min) \
                        .then_inc(S["logit_ready"], 1)

                def weigh(s, b, r):
                    g = group_at(s)
                    slot = dve.snap(g % RING, min_val=0, max_val=RING - 1)
                    dve.wait_ge(S["weight_ready"], before + s + 1)
                    V.tensor_tensor(msg_heads[:, b, :, :, 0:HID],
                                    rows[:, ds(slot, 1), :, 0:D].rearrange("p a k (h c) -> p (a k) h c", h=HEADS),
                                    msg_heads[:, b, :, :, HID:HID + 1].to_broadcast([P, K, HEADS, HID]), ALU.mult) \
                        .then_inc(S["weighted"], 1)

                def gat_one_hot(s, b, r):
                    one_hot(s, b, S["g_agg"], S["gat_onehot"],
                            before + s - (UNROLL - 1) if layer or past(s, UNROLL) else None, 0)

                def update_sums(s, b, r):
                    w = window_at(s)
                    dve.wait_ge(S["g_agg"], before + s + 1)
                    dve.wait_ge(S["shrink_ready"], before + s + 1)
                    if layer or past(s, 1):
                        dve.wait_ge(S["g_acc1"], before + s)
                    for h in range(HEADS):
                        to = acc_heads[:, ds(w, 1), h, :].rearrange("p a c -> p (a c)")
                        ins = V.scalar_tensor_tensor(out=to, in0=to, scalar=shrink[:, b, h:h + 1],
                                                     in1=agg_ps[b % 2][:, h * (HID + 1):(h + 1) * (HID + 1)],
                                                     op0=ALU.mult, op1=ALU.add)
                    ins.then_inc(S["g_acc1"], 1)

                run_steps(dve, [(update_sums, 6), (window_max, 1), (weigh, 4), (gat_one_hot, 4), (logits, 3)])
                dve.wait_ge(S["g_acc1"], before + STEPS)

                bias = vec[:, (GB1, GB2)[layer], :]
                each = 4 + (STAGE_OWN if layer == 0 else 1)
                with own.loop(0, CHUNKS, each) as c:
                    at = ds(c * CH, CH)
                    own(V.reciprocal(gat_stats[:, :, :], acc_heads[:, at, :, HID]))
                    own(V.tensor_tensor(T1.rearrange("p w (h c) -> p w h c", h=HEADS), acc_heads[:, at, :, 0:HID],
                                        gat_stats[:, :, :, None].to_broadcast([P, CH, HEADS, HID]), ALU.mult))
                    own(V.tensor_tensor(T1, T1, all_windows(bias), ALU.add))
                    V.tensor_scalar(T2, T1, 0.0, None, ALU.min).then_inc(S["elu_arg"], 1)
                    dve.wait_ge(S["elu_exp"], c + layer * CHUNKS + 1)
                    own(V.scalar_tensor_tensor(out=FEAT, in0=T2, scalar=-1.0, in1=T1, op0=ALU.add, op1=ALU.max))
                    if layer == 0:
                        V.sem_inc(S["feat_ready"], 1)
                        stage_rows(c, 2 * CHUNKS)
                    else:
                        own(V.tensor_tensor(x_sb[:, at, :], x_sb[:, at, :], FEAT, ALU.add))
                        V.sem_inc(S["out_staged"], 1)


_INS = ["x", "src", "dst", "edge_attr_128", "L0_gnn_w1", "L0_gnn_b1", "L0_gnn_we", "L0_gnn_be", "L0_gnn_eps",
        "L0_gnn_gn_weight", "L0_gnn_gn_bias", "L0_gnn_gn_mean_scale", "L1_gnn_W1", "L1_gnn_a_src1",
        "L1_gnn_a_dst1", "L1_gnn_b1", "L1_gnn_W2", "L1_gnn_a_src2", "L1_gnn_a_dst2", "L1_gnn_b2"]


def kernel(**inputs):
    import numpy as _np
    import concourse.bacc as _bacc
    from concourse import mybir as _mybir
    from concourse.bass_utils import run_bass_kernel_spmd as _run

    nc = _bacc.Bacc("TRN2", target_bir_lowering=False, num_devices=1)
    arrays, args = {}, []
    for name in _INS:
        a = _np.ascontiguousarray(inputs[name])
        if name == "L0_gnn_eps":
            a = a.reshape(1, 1)
        arrays[f"in_{name}"] = a
        args.append(nc.dram_tensor(f"in_{name}", a.shape, _mybir.dt.from_np(a.dtype), kind="ExternalInput").ap())
    out = nc.dram_tensor("out", (N, D), F32, kind="ExternalOutput").ap()
    gnn_kernel(nc, *args, out)
    r = _run(nc, [arrays], core_ids=[0])
    return r.results[0]["out"]
```
